# Optimizing a Trainium2 kernel written in Bass

```python
import numpy as np
import jax
import jax.numpy as jnp

def _softmax(x, axis=-1):
    return jax.nn.softmax(x, axis=axis)

def _gelu(x):
    return jax.nn.gelu(x, approximate=True)

def _silu(x):
    return jax.nn.silu(x)

def _sigmoid(x):
    return jax.nn.sigmoid(x)

def _layernorm(x, axis=-1, eps=1e-05):
    m = jnp.mean(x, axis=axis, keepdims=True)
    v = jnp.var(x, axis=axis, keepdims=True)
    return (x - m) / jnp.sqrt(v + eps)

def _scatter_add(tgt, idx, src, axis=0):
    return tgt.at[idx].add(src)

def _segment_sum(src, seg, n):
    return jax.ops.segment_sum(src, seg, n)
kernel_name = 'mk_dlrm_tower_d1_rec_r8_207e86'

def setup_inputs(seed: int=0):
    np.random.seed(seed)
    _w = jnp.asarray

    def _rec_inputs():
        import jax
        import jax.numpy as jnp
        _tk = jax.random.key(seed)
        ids = jnp.stack([jax.random.randint(jax.random.fold_in(_tk, 200 + f), (512,), 0, v, jnp.int32) for f, v in enumerate([12500, 125000, 12500, 12500, 1250, 1000, 1000, 1250, 1000, 1250, 1000, 1250, 12500, 12500, 1000, 1250, 1000, 1250, 1000, 1000, 1000, 1250, 1000, 12500, 1000, 1250])], axis=1)
        tbl_0 = 0.05 * jax.random.normal(jax.random.fold_in(_tk, 500 + 0), (12500, 128), jnp.float32)
        tbl_1 = 0.05 * jax.random.normal(jax.random.fold_in(_tk, 500 + 1), (125000, 128), jnp.float32)
        tbl_2 = 0.05 * jax.random.normal(jax.random.fold_in(_tk, 500 + 2), (12500, 128), jnp.float32)
        tbl_3 = 0.05 * jax.random.normal(jax.random.fold_in(_tk, 500 + 3), (12500, 128), jnp.float32)
        tbl_4 = 0.05 * jax.random.normal(jax.random.fold_in(_tk, 500 + 4), (1250, 128), jnp.float32)
        tbl_5 = 0.05 * jax.random.normal(jax.random.fold_in(_tk, 500 + 5), (1000, 128), jnp.float32)
        tbl_6 = 0.05 * jax.random.normal(jax.random.fold_in(_tk, 500 + 6), (1000, 128), jnp.float32)
        tbl_7 = 0.05 * jax.random.normal(jax.random.fold_in(_tk, 500 + 7), (1250, 128), jnp.float32)
        tbl_8 = 0.05 * jax.random.normal(jax.random.fold_in(_tk, 500 + 8), (1000, 128), jnp.float32)
        tbl_9 = 0.05 * jax.random.normal(jax.random.fold_in(_tk, 500 + 9), (1250, 128), jnp.float32)
        tbl_10 = 0.05 * jax.random.normal(jax.random.fold_in(_tk, 500 + 10), (1000, 128), jnp.float32)
        tbl_11 = 0.05 * jax.random.normal(jax.random.fold_in(_tk, 500 + 11), (1250, 128), jnp.float32)
        tbl_12 = 0.05 * jax.random.normal(jax.random.fold_in(_tk, 500 + 12), (12500, 128), jnp.float32)
        tbl_13 = 0.05 * jax.random.normal(jax.random.fold_in(_tk, 500 + 13), (12500, 128), jnp.float32)
        tbl_14 = 0.05 * jax.random.normal(jax.random.fold_in(_tk, 500 + 14), (1000, 128), jnp.float32)
        tbl_15 = 0.05 * jax.random.normal(jax.random.fold_in(_tk, 500 + 15), (1250, 128), jnp.float32)
        tbl_16 = 0.05 * jax.random.normal(jax.random.fold_in(_tk, 500 + 16), (1000, 128), jnp.float32)
        tbl_17 = 0.05 * jax.random.normal(jax.random.fold_in(_tk, 500 + 17), (1250, 128), jnp.float32)
        tbl_18 = 0.05 * jax.random.normal(jax.random.fold_in(_tk, 500 + 18), (1000, 128), jnp.float32)
        tbl_19 = 0.05 * jax.random.normal(jax.random.fold_in(_tk, 500 + 19), (1000, 128), jnp.float32)
        tbl_20 = 0.05 * jax.random.normal(jax.random.fold_in(_tk, 500 + 20), (1000, 128), jnp.float32)
        tbl_21 = 0.05 * jax.random.normal(jax.random.fold_in(_tk, 500 + 21), (1250, 128), jnp.float32)
        tbl_22 = 0.05 * jax.random.normal(jax.random.fold_in(_tk, 500 + 22), (1000, 128), jnp.float32)
        tbl_23 = 0.05 * jax.random.normal(jax.random.fold_in(_tk, 500 + 23), (12500, 128), jnp.float32)
        tbl_24 = 0.05 * jax.random.normal(jax.random.fold_in(_tk, 500 + 24), (1000, 128), jnp.float32)
        tbl_25 = 0.05 * jax.random.normal(jax.random.fold_in(_tk, 500 + 25), (1250, 128), jnp.float32)
        _rk = jax.random.fold_in(_tk, 7)
        r_dense_features = -0.000520686 + 1.00062 * jax.random.normal(jax.random.fold_in(_rk, 101), (512, 128), jnp.float32)
        W_top1 = 0.0405887 * jax.random.normal(jax.random.fold_in(_tk, 801), (607, 512), jnp.float32)
        W_top2 = 0.0441942 * jax.random.normal(jax.random.fold_in(_tk, 802), (512, 256), jnp.float32)
        W_top3 = 0.0625 * jax.random.normal(jax.random.fold_in(_tk, 803), (256, 1), jnp.float32)
        b_top1 = jnp.zeros((512,), jnp.float32)
        b_top2 = jnp.zeros((256,), jnp.float32)
        return (r_dense_features, ids, tbl_0, tbl_1, tbl_2, tbl_3, tbl_4, tbl_5, tbl_6, tbl_7, tbl_8, tbl_9, tbl_10, tbl_11, tbl_12, tbl_13, tbl_14, tbl_15, tbl_16, tbl_17, tbl_18, tbl_19, tbl_20, tbl_21, tbl_22, tbl_23, tbl_24, tbl_25, W_top1, b_top1, W_top2, b_top2, W_top3)
    r_dense_features, ids, tbl_0, tbl_1, tbl_2, tbl_3, tbl_4, tbl_5, tbl_6, tbl_7, tbl_8, tbl_9, tbl_10, tbl_11, tbl_12, tbl_13, tbl_14, tbl_15, tbl_16, tbl_17, tbl_18, tbl_19, tbl_20, tbl_21, tbl_22, tbl_23, tbl_24, tbl_25, W_top1, b_top1, W_top2, b_top2, W_top3 = _rec_inputs()

    def _L0_rec_setup():
        import jax, jax.numpy as jnp
        import numpy as np
        F = 26
        B, D = (2048, 128)
        _IU0, _IU1 = np.triu_indices(F + 1, k=1)
        _IU0 = jnp.asarray(_IU0)
        _IU1 = jnp.asarray(_IU1)
        key = jax.random.key(seed)
        k1, k2 = jax.random.split(key)
        dense_features = jax.random.normal(k1, (B, D), dtype=jnp.float32)
        sparse_features = jax.random.normal(k2, (B, F, D), dtype=jnp.float32)
        return {'dense_features': dense_features, 'sparse_features': sparse_features}
    _L0_rec_all = _L0_rec_setup()
    _L0_rec_in = {k: v for k, v in _L0_rec_all.items() if k in ()}
    del _L0_rec_all
    return {'r_dense_features': r_dense_features, 'ids': ids, 'tbl_0': tbl_0, 'tbl_1': tbl_1, 'tbl_2': tbl_2, 'tbl_3': tbl_3, 'tbl_4': tbl_4, 'tbl_5': tbl_5, 'tbl_6': tbl_6, 'tbl_7': tbl_7, 'tbl_8': tbl_8, 'tbl_9': tbl_9, 'tbl_10': tbl_10, 'tbl_11': tbl_11, 'tbl_12': tbl_12, 'tbl_13': tbl_13, 'tbl_14': tbl_14, 'tbl_15': tbl_15, 'tbl_16': tbl_16, 'tbl_17': tbl_17, 'tbl_18': tbl_18, 'tbl_19': tbl_19, 'tbl_20': tbl_20, 'tbl_21': tbl_21, 'tbl_22': tbl_22, 'tbl_23': tbl_23, 'tbl_24': tbl_24, 'tbl_25': tbl_25, 'W_top1': W_top1, 'b_top1': b_top1, 'W_top2': W_top2, 'b_top2': b_top2, 'W_top3': W_top3}

def reference(r_dense_features, ids, tbl_0, tbl_1, tbl_2, tbl_3, tbl_4, tbl_5, tbl_6, tbl_7, tbl_8, tbl_9, tbl_10, tbl_11, tbl_12, tbl_13, tbl_14, tbl_15, tbl_16, tbl_17, tbl_18, tbl_19, tbl_20, tbl_21, tbl_22, tbl_23, tbl_24, tbl_25, W_top1, b_top1, W_top2, b_top2, W_top3):
    import jax
    import jax.numpy as jnp

    def _L0_rec_ref(dense_features, sparse_features):
        import jax, jax.numpy as jnp
        import numpy as np
        F = 26
        B, D = (2048, 128)
        _IU0, _IU1 = np.triu_indices(F + 1, k=1)
        _IU0 = jnp.asarray(_IU0)
        _IU1 = jnp.asarray(_IU1)
        combined = jnp.concatenate([dense_features[:, None, :], sparse_features], axis=1)
        interactions = jnp.einsum('bfd,bgd->bfg', combined, combined)
        interactions_flat = interactions[:, _IU0, _IU1]
        return jnp.concatenate([dense_features, interactions_flat], axis=1)
    e = jnp.stack([tbl_0[ids[:, 0]], tbl_1[ids[:, 1]], tbl_2[ids[:, 2]], tbl_3[ids[:, 3]], tbl_4[ids[:, 4]], tbl_5[ids[:, 5]], tbl_6[ids[:, 6]], tbl_7[ids[:, 7]], tbl_8[ids[:, 8]], tbl_9[ids[:, 9]], tbl_10[ids[:, 10]], tbl_11[ids[:, 11]], tbl_12[ids[:, 12]], tbl_13[ids[:, 13]], tbl_14[ids[:, 14]], tbl_15[ids[:, 15]], tbl_16[ids[:, 16]], tbl_17[ids[:, 17]], tbl_18[ids[:, 18]], tbl_19[ids[:, 19]], tbl_20[ids[:, 20]], tbl_21[ids[:, 21]], tbl_22[ids[:, 22]], tbl_23[ids[:, 23]], tbl_24[ids[:, 24]], tbl_25[ids[:, 25]]], axis=1)
    z = _L0_rec_ref(r_dense_features, e)
    z = z.reshape(z.shape[0], -1)
    h = jnp.concatenate([z, r_dense_features], axis=1)
    h = jnp.maximum(h @ W_top1 + b_top1, 0.0)
    h = jnp.maximum(h @ W_top2 + b_top2, 0.0)
    y = h @ W_top3
    return y

_drawn_inputs = setup_inputs


def setup_inputs(seed=0):
    import zlib

    import numpy as np

    out = dict(_drawn_inputs(seed))
    spreads = {'b_top1': (0.0, 0.1), 'b_top2': (0.0, 0.1)}
    factors = {}
    for name, (base, spread) in spreads.items():
        noise = np.random.default_rng([zlib.crc32(name.encode()), seed]).standard_normal(out[name].shape)
        drawn = base * np.exp(spread * noise) if base else spread * noise
        out[name] = jnp.asarray(drawn.astype(out[name].dtype))
    for name, factor in factors.items():
        out[name] = (out[name] * factor).astype(out[name].dtype)
    return out
```

```python
import concourse.bass as bass
from concourse import mybir
from contextlib import ExitStack

TABLES = 26
FEATURES = TABLES + 1
SHIFTS = (FEATURES + 1) // 2
P = 128


def pair_places():
    seen, places = set(), []
    for feature in range(FEATURES):
        for shift in range(1, SHIFTS + 1):
            a, b = divmod(feature * FEATURES + feature + shift, FEATURES)
            low, high = min(a, b), max(a, b)
            if a >= FEATURES or (low, high) in seen:
                places.append(None)
            else:
                seen.add((low, high))
                places.append(low * FEATURES - low * (low + 1) // 2 + high - low - 1)
    assert len(seen) == FEATURES * (FEATURES - 1) // 2
    return places


def build_tower(nc, dense_t, ids_by_sample, tables, w1_dense, w1_pairs, b1_cols, w2_rows, b2_cols, w3_cols, out):
    fp32 = mybir.dt.float32
    ALU = mybir.AluOpType
    ACT = mybir.ActivationFunctionType

    D, B = dense_t.shape
    H1 = w1_dense.shape[2]
    H2 = w2_rows.shape[2]
    M1, M2 = H1 // P, H2 // P
    CHUNKS = B // P
    STRIPS, COLS = 4, 32
    SLOTS = P // STRIPS
    BLOCKS = 3
    PER_BLOCK = FEATURES // BLOCKS
    PAIR_P = PER_BLOCK * SHIFTS
    SQUARE = FEATURES + 1

    SIZES = [4, 4, 3, 3, 3, 3, 3, 3]
    GROUPS = len(SIZES)
    STARTS = [sum(SIZES[:g]) for g in range(GROUPS)]
    GROUP_OF = [g for g in range(GROUPS) for _ in range(SIZES[g])]
    FILLS, FILL_COLS = 4, 8
    HALF = GROUPS // 2

    ctx = ExitStack()
    with ctx:
        def sb(name, shape, dt=fp32):
            return ctx.enter_context(nc.sbuf_tensor(name, shape, dt))

        def pb(name, shape):
            return ctx.enter_context(nc.psum_tensor(name, shape, fp32))

        def sem(name):
            return ctx.enter_context(nc.semaphore(name))

        ids = sb("ids", [P, CHUNKS * TABLES], mybir.dt.int32)
        rows = sb("rows", [P, TABLES, D])
        feats = sb("feats", [D, P, SLOTS])
        dense = sb("dense", [D, B])
        pairs = sb("pairs", [P, FEATURES, COLS])
        pair_rows = sb("pair_rows", [PAIR_P, BLOCKS, P])
        ident = sb("ident", [P, P])
        w1d = sb("w1d", [D, 2, H1])
        w1d_sum = sb("w1d_sum", [D, H1])
        w1p = sb("w1p", [PAIR_P, BLOCKS, H1])
        w2 = sb("w2", [P, M1, H2])
        w3 = sb("w3", [P, M2])
        b1 = sb("b1", [P, M1])
        b2 = sb("b2", [P, M2])
        h1 = sb("h1", [P, M1, P])
        h2 = sb("h2", [P, M2, P])
        y = sb("y", [1, B])
        scratch = nc.dram_tensor("pairs_scratch", (SQUARE, FEATURES, P), fp32, kind="Internal").ap()

        turned = [pb(f"turned{i}", [D, 4, P]) for i in range(2)]
        gram = [pb(f"gram{i}", [P, FILL_COLS, STRIPS, SLOTS]) for i in range(2)]
        mlp = [pb(f"mlp{i}", [P, 4, P]) for i in range(2)]

        ids_in = sem("ids_in")
        dense_in = sem("dense_in")
        w1d_in = sem("w1d_in")
        w1p_in = sem("w1p_in")
        w2_in = sem("w2_in")
        small_in = sem("small_in")
        ident_done = sem("ident_done")
        slots_zeroed = sem("slots_zeroed")
        w1_summed = sem("w1_summed")
        gathered = [sem(f"gathered{f}") for f in range(TABLES)]
        group_turned = sem("group_turned")
        feats_act = sem("feats_act")
        feats_dve = sem("feats_dve")
        dense_placed = sem("dense_placed")
        fill_done = sem("fill_done")
        pairs_act = sem("pairs_act")
        pairs_dve = sem("pairs_dve")
        pairs_out = sem("pairs_out")
        pairs_in = sem("pairs_in")
        layer1_done = sem("layer1_done")
        h1_act = sem("h1_act")
        h1_dve = sem("h1_dve")
        layer2_done = sem("layer2_done")
        h2_act = sem("h2_act")
        h2_dve = sem("h2_dve")
        layer3_done = sem("layer3_done")
        y_done = sem("y_done")
        out_stored = sem("out_stored")

        block = ctx.enter_context(nc.Block())

        def store_strip(engine, strip):
            engine.dma_start(scratch[:, :, strip * COLS:(strip + 1) * COLS],
                             pairs[SLOTS * strip:SLOTS * strip + SQUARE, :, :]).then_inc(pairs_out, 16)

        @block.sync
        def _(sp):
            sp.dma_start(ids[:, :], ids_by_sample).then_inc(ids_in, 16)
            sp.dma_start(dense[:, :], dense_t).then_inc(dense_in, 16)
            sp.dma_start(w1p[:, :, :], w1_pairs).then_inc(w1p_in, 16)
            sp.dma_start(w1d[:, :, :], w1_dense).then_inc(w1d_in, 16)
            sp.dma_start(w2[:, :, :], w2_rows).then_inc(w2_in, 16)

            def load_pairs():
                for j in range(BLOCKS):
                    source = bass.AP(scratch.tensor, (PER_BLOCK * j * (FEATURES + 1) + 1) * P,
                                     [[(FEATURES + 1) * P, PER_BLOCK], [P, SHIFTS], [1, P]])
                    sp.dma_start(pair_rows[:, j, :], source).then_inc(pairs_in, 16)

            sp.wait_ge(pairs_dve, FILLS)
            for strip in (2, 3):
                store_strip(sp, strip)
            sp.wait_ge(pairs_out, 16 * STRIPS)
            load_pairs()
            with sp.Fori(1, CHUNKS) as c:
                fills = sp.snap(FILLS * c + FILLS)
                stores = sp.snap(16 * STRIPS * c + 16 * STRIPS)
                loads_before = sp.snap(16 * BLOCKS * c)
                layer1_before = sp.snap(2 * c)
                sp.wait_ge(pairs_in, loads_before)
                sp.wait_ge(pairs_dve, fills)
                for strip in (2, 3):
                    store_strip(sp, strip)
                sp.wait_ge(layer1_done, layer1_before)
                sp.wait_ge(pairs_out, stores)
                load_pairs()
            sp.wait_ge(y_done, 1 + CHUNKS)
            sp.dma_start(out, y[:, :]).then_inc(out_stored, 16)
            sp.wait_ge(out_stored, 16)

        @block.gpsimd
        def _(pool):
            pool.wait_ge(ids_in, 16)
            for c in range(CHUNKS):
                for f in range(TABLES):
                    if c >= 1:
                        pool.wait_ge(group_turned, GROUPS * (c - 1) + GROUP_OF[f] + 1)
                    col = c * TABLES + f
                    pool.indirect_dma_start(
                        rows[:, f, :], None, tables[f],
                        bass.IndirectOffsetOnAxis(ids[:, col:col + 1], 0)).then_inc(gathered[f], 16)
                    if c == 0 and f == 1:
                        pool.memset(ident[:, :], 0.0).then_inc(ident_done, 1)
                        pool.wait_ge(ident_done, 1)
                        pool.affine_select(out=ident[:, :], in_=ident[:, :], compare_op=ALU.not_equal, fill=1.0,
                                           base=0, pattern=[[-1, P]], channel_multiplier=1).then_inc(ident_done, 1)

        def group_to_feats(engine_copy, g):
            lo, n = STARTS[g] + 1, SIZES[g]
            return engine_copy(feats[:, :, lo:lo + n].rearrange("d b f -> d f b"), turned[g % 2][:, 0:n, :])

        def fill_to_pairs(engine_copy, n, s):
            lo = SLOTS * s
            return engine_copy(pairs[lo:lo + SLOTS, :, n * FILL_COLS:(n + 1) * FILL_COLS].rearrange("p f t -> p t f"),
                               gram[n % 2][lo:lo + SLOTS, :, s, 0:FEATURES])

        @block.scalar
        def _(act):
            act.dma_start(b1[:, :], b1_cols).then_inc(small_in, 16)
            act.dma_start(b2[:, :], b2_cols).then_inc(small_in, 16)
            act.dma_start(w3[:, :], w3_cols).then_inc(small_in, 16)

            def collect(c, groups):
                for g in groups:
                    act.wait_ge(group_turned, GROUPS * c + g + 1)
                    if g == 0:
                        act.wait_ge(fill_done, FILLS * c)
                    group_to_feats(nc.scalar.copy, g).then_inc(feats_act, 1)

            def store_first_strips(c):
                act.wait_ge(pairs_act, FILLS * c + FILLS)
                if isinstance(c, int) and c == 0:
                    pass
                else:
                    act.wait_ge(pairs_in, 16 * BLOCKS * c)
                for strip in (0, 1):
                    store_strip(act, strip)

            def diagonals(c):
                for n in range(FILLS):
                    act.wait_ge(fill_done, FILLS * c + n + 1)
                    if n == 0:
                        act.wait_ge(pairs_out, 16 * STRIPS * c)
                    fill_to_pairs(nc.scalar.copy, n, 0)
                    fill_to_pairs(nc.scalar.copy, n, 1).then_inc(pairs_act, 1)
                store_first_strips(c)

            def activate(c):
                act.wait_ge(layer1_done, 2 * c + 1)
                for m in range(M1 // 2):
                    op = nc.scalar.activation(h1[:, m, :], mlp[0][:, m, :], ACT.Relu, bias=b1[:, m:m + 1])
                op.then_inc(h1_act, 1)
                act.wait_ge(layer2_done, 2 * c + 1)
                nc.scalar.activation(h2[:, 0, :], mlp[0][:, 0, :], ACT.Relu, bias=b2[:, 0:1]).then_inc(h2_act, 1)
                act.wait_ge(layer3_done, c + 1)
                nc.scalar.copy(y[0:1, bass.ds(c * P, P)], mlp[0][0:1, 0, :]).then_inc(y_done, 1)

            act.sem_inc(y_done, 1)
            for g in range(0, GROUPS, 2):
                act.wait_ge(group_turned, g + 1)
                group_to_feats(nc.scalar.copy, g).then_inc(feats_act, 1)
            for n in range(FILLS):
                act.wait_ge(fill_done, n + 1)
                fill_to_pairs(nc.scalar.copy, n, 0)
                fill_to_pairs(nc.scalar.copy, n, 1).then_inc(pairs_act, 1)
            store_first_strips(0)
            act.wait_ge(small_in, 48)
            with act.Fori(1, CHUNKS) as c:
                collect(c, range(0, HALF, 2))
                activate(c - 1)
                collect(c, range(HALF, GROUPS, 2))
                diagonals(c)
            activate(CHUNKS - 1)

        @block.vector
        def _(dve):
            def place_dense(c):
                now = dense[:, bass.ds(c * P, P)].rearrange("d (s t) -> d t s", s=STRIPS)
                nc.vector.tensor_copy(feats[:, :, 0].rearrange("d (t s) -> d t s", s=STRIPS),
                                      now).then_inc(dense_placed, 1)

            def rectify(c):
                dve.wait_ge(layer1_done, 2 * c + 2)
                for m in range(M1 // 2, M1):
                    op = nc.vector.tensor_scalar(h1[:, m, :], mlp[1][:, m - M1 // 2, :], b1[:, m:m + 1], 0.0,
                                                 ALU.add, ALU.max)
                op.then_inc(h1_dve, 1)
                dve.wait_ge(layer2_done, 2 * c + 2)
                nc.vector.tensor_scalar(h2[:, 1, :], mlp[1][:, 0, :], b2[:, 1:2], 0.0,
                                        ALU.add, ALU.max).then_inc(h2_dve, 1)

            nc.vector.memset(feats[:, :, FEATURES:SLOTS], 0.0).then_inc(slots_zeroed, 1)
            dve.wait_ge(dense_in, 16)
            place_dense(0)
            for g in range(1, GROUPS, 2):
                dve.wait_ge(group_turned, g + 1)
                group_to_feats(nc.vector.tensor_copy, g).then_inc(feats_dve, 1)
            dve.wait_ge(w1d_in, 16)
            nc.vector.tensor_tensor(w1d_sum[:, :], w1d[:, 0, :], w1d[:, 1, :], ALU.add).then_inc(w1_summed, 1)
            for n in range(FILLS):
                dve.wait_ge(fill_done, n + 1)
                fill_to_pairs(nc.vector.tensor_copy, n, 2)
                fill_to_pairs(nc.vector.tensor_copy, n, 3).then_inc(pairs_dve, 1)
            dve.wait_ge(small_in, 48)
            with dve.Fori(1, CHUNKS) as c:
                dve.wait_ge(fill_done, FILLS * c)
                place_dense(c)
                for g in range(1, HALF, 2):
                    dve.wait_ge(group_turned, GROUPS * c + g + 1)
                    group_to_feats(nc.vector.tensor_copy, g).then_inc(feats_dve, 1)
                rectify(c - 1)
                for g in range(HALF + 1, GROUPS, 2):
                    dve.wait_ge(group_turned, GROUPS * c + g + 1)
                    group_to_feats(nc.vector.tensor_copy, g).then_inc(feats_dve, 1)
                for n in range(FILLS):
                    dve.wait_ge(fill_done, FILLS * c + n + 1)
                    if n == 0:
                        dve.wait_ge(pairs_out, 16 * STRIPS * c)
                    fill_to_pairs(nc.vector.tensor_copy, n, 2)
                    fill_to_pairs(nc.vector.tensor_copy, n, 3).then_inc(pairs_dve, 1)
            rectify(CHUNKS - 1)

        @block.tensor
        def _(pe):
            def turn(c, g):
                for i in range(SIZES[g]):
                    pe.wait_ge(gathered[STARTS[g] + i], 16 * c + 16)
                    op = nc.tensor.transpose(turned[g % 2][:, i, :], rows[:, STARTS[g] + i, :], ident[:, :])
                op.then_inc(group_turned, 1)

            def grams(c, first):
                pe.wait_ge(feats_act, (GROUPS // 2) * c + GROUPS // 2)
                pe.wait_ge(feats_dve, (GROUPS // 2) * c + GROUPS // 2)
                pe.wait_ge(dense_placed, c + 1)
                by_col = feats[:, :, :].rearrange("d (t s) f -> d t (s f)", s=STRIPS)
                for n in range(FILLS):
                    if n >= 2 or not first:
                        pe.wait_ge(pairs_act, FILLS * c + n - 1)
                        pe.wait_ge(pairs_dve, FILLS * c + n - 1)
                    for k in range(FILL_COLS):
                        four = by_col[:, n * FILL_COLS + k, :]
                        used = four.rearrange("d (s f) -> d s f", s=STRIPS)[:, :, 0:FEATURES]
                        op = nc.tensor.matmul(gram[n % 2][:, k, :, 0:FEATURES], four, used,
                                              start=True, stop=True)
                    op.then_inc(fill_done, 1)

            def tower(c):
                x_dense = dense[:, bass.ds(c * P, P)]
                pe.wait_ge(y_done, c + 1)
                pe.wait_ge(pairs_in, 16 * BLOCKS * c + 16 * BLOCKS)
                for m in range(M1):
                    units = slice(m * P, (m + 1) * P)
                    acc = mlp[m // 2][:, m % 2, :]
                    nc.tensor.matmul(acc, w1d_sum[:, units], x_dense, start=True, stop=False)
                    for j in range(BLOCKS):
                        op = nc.tensor.matmul(acc, w1p[:, j, units], pair_rows[:, j, :],
                                              start=False, stop=(j == BLOCKS - 1))
                    if m % 2:
                        op.then_inc(layer1_done, 1)
                pe.wait_ge(h1_act, c + 1)
                pe.wait_ge(h1_dve, c + 1)
                for m in range(M2):
                    for k in range(M1):
                        op = nc.tensor.matmul(mlp[m][:, 0, :], w2[:, k, m * P:(m + 1) * P], h1[:, k, :],
                                              start=(k == 0), stop=(k == M1 - 1))
                    op.then_inc(layer2_done, 1)
                pe.wait_ge(h2_act, c + 1)
                pe.wait_ge(h2_dve, c + 1)
                for k in range(M2):
                    op = nc.tensor.matmul(mlp[0][0:1, 0, :], w3[:, k:k + 1], h2[:, k, :],
                                          start=(k == 0), stop=(k == M2 - 1))
                op.then_inc(layer3_done, 1)

            def bank_free(c, g, first=False):
                if g % 2 == 0:
                    if not (first and g < 2):
                        pe.wait_ge(feats_act, (GROUPS // 2) * c + g // 2)
                else:
                    if not (first and g < 2):
                        pe.wait_ge(feats_dve, (GROUPS // 2) * c + g // 2)

            pe.wait_ge(ident_done, 2)
            for g in range(GROUPS):
                bank_free(0, g, first=True)
                turn(0, g)
            pe.wait_ge(slots_zeroed, 1)
            grams(0, first=True)
            pe.wait_ge(w1_summed, 1)
            pe.wait_ge(w1p_in, 16)
            pe.wait_ge(w2_in, 16)
            pe.wait_ge(small_in, 48)
            with pe.Fori(1, CHUNKS) as c:
                for g in range(HALF):
                    bank_free(c, g)
                    turn(c, g)
                tower(c - 1)
                for g in range(HALF, GROUPS):
                    bank_free(c, g)
                    turn(c, g)
                grams(c, first=False)
            tower(CHUNKS - 1)


def kernel(**inputs):
    import numpy as np
    import concourse.bacc as bacc
    from concourse import mybir
    from concourse.bass_utils import run_bass_kernel_spmd

    w1 = np.asarray(inputs["W_top1"])
    w2 = np.asarray(inputs["W_top2"])
    x = np.asarray(inputs["r_dense_features"])
    ids = np.asarray(inputs["ids"])
    batch, d = x.shape
    n_pairs = FEATURES * (FEATURES - 1) // 2
    h1, h2 = w2.shape
    w1_places = np.stack([np.zeros_like(w1[0]) if row is None else w1[d + row] for row in pair_places()])
    arrays = {
        "dense_t": x.T,
        "ids": ids.reshape(batch // P, 4, P // 4, TABLES).transpose(2, 1, 0, 3).reshape(P, -1),
        "w1_dense": np.stack([w1[0:d], w1[d + n_pairs:]], axis=1),
        "w1_pairs": w1_places.reshape(3, -1, h1).transpose(1, 0, 2),
        "b1": np.asarray(inputs["b_top1"]).reshape(h1 // P, P).T,
        "w2": w2.reshape(h1 // P, P, h2).transpose(1, 0, 2),
        "b2": np.asarray(inputs["b_top2"]).reshape(h2 // P, P).T,
        "w3": np.asarray(inputs["W_top3"]).reshape(h2 // P, P).T,
    }
    for f in range(TABLES):
        arrays[f"tbl_{f}"] = np.asarray(inputs[f"tbl_{f}"])
    arrays = {f"in_{name}": np.ascontiguousarray(a) for name, a in arrays.items()}

    nc = bacc.Bacc("TRN2", target_bir_lowering=False, num_devices=1)
    aps = {name[3:]: nc.dram_tensor(name, a.shape, mybir.dt.from_np(a.dtype), kind="ExternalInput").ap()
           for name, a in arrays.items()}
    out = nc.dram_tensor("out", (1, batch), mybir.dt.float32, kind="ExternalOutput").ap()
    build_tower(nc, aps["dense_t"], aps["ids"], [aps[f"tbl_{f}"] for f in range(TABLES)], aps["w1_dense"],
                aps["w1_pairs"], aps["b1"], aps["w2"], aps["b2"], aps["w3"], out)
    result = run_bass_kernel_spmd(nc, [arrays], core_ids=[0])
    return result.results[0]["out"].reshape(batch, 1)
```

```python
import concourse.bass as bass
from concourse import mybir
from contextlib import ExitStack

SELECTED = [5, 6, 8, 10, 14, 16, 18, 19]
ROWS_SELECTED = 1000
TABLES = 26
GATHERED = [f for f in range(TABLES) if f not in SELECTED]
FEATURES = TABLES + 1
SLOT_FEATURES = [0] + [1 + f for f in GATHERED + SELECTED]
SHIFTS = (FEATURES + 1) // 2
P = 128
STRIPS = 4


def pair_places():
    seen, places = set(), []
    for slot in range(FEATURES):
        for shift in range(1, SHIFTS + 1):
            a, b = divmod(slot * FEATURES + slot + shift, FEATURES)
            if a >= FEATURES or (min(a, b), max(a, b)) in seen:
                places.append(None)
                continue
            seen.add((min(a, b), max(a, b)))
            low, high = sorted((SLOT_FEATURES[a], SLOT_FEATURES[b]))
            places.append(low * FEATURES - low * (low + 1) // 2 + high - low - 1)
    assert len(seen) == FEATURES * (FEATURES - 1) // 2
    return places


def build_tower(nc, dense_t, ids_gather, ids_select, tables, table_rows, w1_dense, w1_pairs, b1_cols,
                w2_rows, b2_cols, w3_cols, out):
    fp32 = mybir.dt.float32
    fp32r = mybir.dt.float32r
    int32 = mybir.dt.int32
    ALU = mybir.AluOpType
    ACT = mybir.ActivationFunctionType

    D, B = dense_t.shape
    H1 = w1_dense.shape[2]
    H2 = w2_rows.shape[2]
    M1, M2 = H1 // P, H2 // P
    CHUNKS = B // P
    COLS = P // STRIPS
    SLOTS = P // STRIPS
    BLOCKS = 3
    PER_BLOCK = FEATURES // BLOCKS
    PAIR_P = PER_BLOCK * SHIFTS
    SQUARE = FEATURES + 1
    NG, NS = len(GATHERED), len(SELECTED)
    KS = table_rows.shape[2]

    STARTS = list(range(0, NG, 4))
    SIZES = [min(4, NG - s) for s in STARTS]
    GROUPS = len(SIZES)
    FILLS, FILL_COLS = 4, 8
    turns = [(c, g) for c in range(CHUNKS) for g in range(GROUPS)]
    index_of = {cg: n for n, cg in enumerate(turns)}
    FIRST_GRAM = max(NS - 1, GROUPS)
    FIRST_PART = 2
    RAW = 3

    ctx = ExitStack()
    with ctx:
        def sb(name, shape, dt=fp32):
            return ctx.enter_context(nc.sbuf_tensor(name, shape, dt))

        def pb(name, shape):
            return ctx.enter_context(nc.psum_tensor(name, shape, fp32))

        def sem(name):
            return ctx.enter_context(nc.semaphore(name))

        ids = sb("ids", [P, CHUNKS * NG], int32)
        ids_rep = sb("ids_rep", [P, RAW, B], int32)
        row_int = sb("row_int", [P, KS], int32)
        row_id = sb("row_id", [P, KS])
        select = [sb(f"select{i}", [P, KS, B], fp32r) for i in range(2)]
        table = sb("table", [P, RAW, KS, D])
        table_hi = [sb(f"table_hi{i}", [P, KS, D], fp32r) for i in range(2)]
        table_lo = [sb(f"table_lo{i}", [P, KS, D], fp32r) for i in range(2)]
        rows = sb("rows", [P, 2, NG, D])
        feats = sb("feats", [D, B, SLOTS])
        dense = sb("dense", [D, B])
        pairs = sb("pairs", [P, FEATURES, COLS])
        pair_rows = sb("pair_rows", [PAIR_P, BLOCKS, P])
        ident = sb("ident", [P, P])
        w1d = sb("w1d", [D, 2, H1])
        w1d_sum = sb("w1d_sum", [D, H1])
        w1p = sb("w1p", [PAIR_P, BLOCKS, H1])
        w2 = sb("w2", [P, M1, H2])
        w3 = sb("w3", [P, M2])
        b1 = sb("b1", [P, M1])
        b2 = sb("b2", [P, M2])
        h1 = sb("h1", [P, M1, P])
        h2 = sb("h2", [P, M2, P])
        y = sb("y", [1, B])
        scratch = nc.dram_tensor("pairs_scratch", (SQUARE, FEATURES, P), fp32, kind="Internal").ap()

        turned = [pb(f"turned{i}", [D, 4, P]) for i in range(2)]
        gram = [pb(f"gram{i}", [P, FILL_COLS, STRIPS, SLOTS]) for i in range(2)]
        mlp = [pb(f"mlp{i}", [P, 4, P]) for i in range(2)]
        looked_up = [gram[i // 2][:, 4 * (i % 2):4 * (i % 2) + 4, :, :].rearrange("p k s f -> p (k s f)")
                     for i in range(4)]

        ids_in = sem("ids_in")
        dense_in = sem("dense_in")
        ids_rep_in = [sem(f"ids_rep_in{i}") for i in range(RAW)]
        table_in = [sem(f"table_in{i}") for i in range(RAW)]
        w1d_in = sem("w1d_in")
        w1p_in = sem("w1p_in")
        w2_in = sem("w2_in")
        small_in = sem("small_in")
        ident_done = sem("ident_done")
        row_int_done = sem("row_int_done")
        row_id_done = sem("row_id_done")
        slots_zeroed = sem("slots_zeroed")
        w1_summed = sem("w1_summed")
        gathered = [[sem(f"gathered{half}_{n}") for n in range(NG)] for half in range(2)]
        hi_done = sem("hi_done")
        lo_done = sem("lo_done")
        select_done = sem("select_done")
        table_used = sem("table_used")
        table_placed = sem("table_placed")
        group_turned = sem("group_turned")
        group_placed = sem("group_placed")
        dense_placed = sem("dense_placed")
        fill_done = sem("fill_done")
        pairs_act = sem("pairs_act")
        pairs_dve = sem("pairs_dve")
        pairs_out = sem("pairs_out")
        pairs_in = [sem(f"pairs_in{j}") for j in range(BLOCKS)]
        layer1_done = sem("layer1_done")
        h1_act = sem("h1_act")
        h1_dve = sem("h1_dve")
        layer2_done = sem("layer2_done")
        h2_act = sem("h2_act")
        h2_dve = sem("h2_dve")
        layer3_done = sem("layer3_done")
        y_done = sem("y_done")
        out_stored = sem("out_stored")

        block = ctx.enter_context(nc.Block())

        def store_strip(engine, strip):
            engine.dma_start(scratch[:, :, strip * COLS:(strip + 1) * COLS],
                             pairs[SLOTS * strip:SLOTS * strip + SQUARE, :, :]).then_inc(pairs_out, 16)

        def load_block(engine, j):
            source = bass.AP(scratch.tensor, (PER_BLOCK * j * (FEATURES + 1) + 1) * P,
                             [[(FEATURES + 1) * P, PER_BLOCK], [P, SHIFTS], [1, P]])
            engine.dma_start(pair_rows[:, j, :], source).then_inc(pairs_in[j], 16)

        def fill_to_pairs(engine_copy, n, s):
            lo = SLOTS * s
            return engine_copy(pairs[lo:lo + SLOTS, :, n * FILL_COLS:(n + 1) * FILL_COLS].rearrange("p f t -> p t f"),
                               gram[n % 2][lo:lo + SLOTS, :, s, 0:FEATURES])

        @block.sync
        def _(sp):
            sp.dma_start(ids[:, :], ids_gather).then_inc(ids_in, 16)
            for i in range(NS):
                everywhere = ids_select[i:i + 1, :].broadcast_to([P, B])
                if i >= RAW:
                    sp.wait_ge(lo_done, i - RAW + 1)
                    sp.wait_ge(select_done, KS * (i - RAW + 1))
                sp.dma_start(ids_rep[:, i % RAW, :], everywhere).then_inc(ids_rep_in[i % RAW], 16)
                sp.dma_start(table[:, i % RAW, :, :], table_rows[i]).then_inc(table_in[i % RAW], 16)
                if i == RAW:
                    sp.dma_start(dense[:, :], dense_t).then_inc(dense_in, 16)
            sp.dma_start(w1p[:, :, :], w1_pairs).then_inc(w1p_in, 16)
            sp.dma_start(w1d[:, :, :], w1_dense).then_inc(w1d_in, 16)
            sp.dma_start(w2[:, :, :], w2_rows).then_inc(w2_in, 16)
            sp.dma_start(b1[:, :], b1_cols).then_inc(small_in, 16)
            sp.dma_start(b2[:, :], b2_cols).then_inc(small_in, 16)
            sp.dma_start(w3[:, :], w3_cols).then_inc(small_in, 16)
            for c in range(CHUNKS):
                last = c == CHUNKS - 1
                if c >= 1:
                    for j in range(BLOCKS):
                        sp.wait_ge(pairs_in[j], 16 * c)
                sp.wait_ge(pairs_dve, FILLS * (c + 1))
                for strip in (2, 3):
                    store_strip(sp, strip)
                if not last:
                    sp.wait_ge(pairs_act, FILLS * (c + 1))
                    for strip in (0, 1):
                        store_strip(sp, strip)
                if c >= 1:
                    sp.wait_ge(layer1_done, 2 * c)
                sp.wait_ge(pairs_out, 16 * STRIPS * (c + 1))
                for j in range(BLOCKS):
                    if not last or j != 1:
                        load_block(sp, j)
            sp.wait_ge(y_done, CHUNKS)
            sp.dma_start(out, y[:, :]).then_inc(out_stored, 16)
            sp.wait_ge(out_stored, 16)

        @block.gpsimd
        def _(pool):
            pool.iota(row_int[:, :], [[1, KS]], base=0, channel_multiplier=KS).then_inc(row_int_done, 1)
            pool.memset(ident[:, :], 0.0).then_inc(ident_done, 1)
            pool.wait_ge(ident_done, 1)
            pool.affine_select(out=ident[:, :], in_=ident[:, :], compare_op=ALU.not_equal, fill=1.0,
                               base=0, pattern=[[-1, P]], channel_multiplier=1).then_inc(ident_done, 1)
            pool.wait_ge(ids_in, 16)
            for c in range(CHUNKS):
                for n in range(NG):
                    if c >= 2 and n in STARTS:
                        pool.wait_ge(group_turned, index_of[c - 2, STARTS.index(n)] + 1)
                    col = c * NG + n
                    pool.indirect_dma_start(
                        rows[:, c % 2, n, :], None, tables[GATHERED[n]],
                        bass.IndirectOffsetOnAxis(ids[:, col:col + 1], 0)).then_inc(gathered[c % 2][n], 16)

        @block.scalar
        def _(act):
            def split(i):
                act.wait_ge(table_in[i % RAW], 16 * (i // RAW + 1))
                if i >= 2:
                    act.wait_ge(table_used, i - 1)
                nc.scalar.copy(table_hi[i % 2][:, :, :], table[:, i % RAW, :, :]).then_inc(hi_done, 1)

            def place_table(i):
                act.wait_ge(table_used, i + 1)
                nc.scalar.copy(feats[:, :, 1 + NG + i], looked_up[i % 4]).then_inc(table_placed, 1)

            def place_group(n):
                c, g = turns[n]
                lo, size = STARTS[g] + 1, SIZES[g]
                act.wait_ge(group_turned, n + 1)
                nc.scalar.copy(feats[:, c * P:(c + 1) * P, lo:lo + size].rearrange("d b f -> d f b"),
                               turned[n % 2][:, 0:size, :]).then_inc(group_placed, 1)

            def keep_diagonals(c):
                for n in range(FILLS):
                    act.wait_ge(fill_done, FILLS * c + n + 1)
                    if n == 0 and c >= 1:
                        act.wait_ge(pairs_out, 16 * STRIPS * c)
                    fill_to_pairs(nc.scalar.copy, n, 0)
                    fill_to_pairs(nc.scalar.copy, n, 1).then_inc(pairs_act, 1)

            def activate1(c):
                act.wait_ge(layer1_done, 2 * c + 1)
                for m in range(M1 // 2):
                    op = nc.scalar.activation(h1[:, m, :], mlp[0][:, m, :], ACT.Relu, bias=b1[:, m:m + 1])
                op.then_inc(h1_act, 1)

            def activate2(c):
                act.wait_ge(layer2_done, 2 * c + 1)
                nc.scalar.activation(h2[:, 0, :], mlp[0][:, 0, :], ACT.Relu, bias=b2[:, 0:1]).then_inc(h2_act, 1)
                act.wait_ge(layer3_done, c + 1)
                nc.scalar.copy(y[0:1, c * P:(c + 1) * P], mlp[0][0:1, 0, :]).then_inc(y_done, 1)

            split(0)
            split(1)
            for i in range(max(NS, FIRST_GRAM + 1)):
                if i < NS:
                    place_table(i)
                if i + 2 < NS:
                    split(i + 2)
                if i >= 1:
                    place_group(i - 1)
            keep_diagonals(0)
            act.wait_ge(small_in, 48)
            for c in range(1, CHUNKS):
                for g in range(GROUPS):
                    if c >= 2 and g == FIRST_PART:
                        activate1(c - 2)
                    if index_of[c, g] >= FIRST_GRAM:
                        place_group(index_of[c, g])
                if c >= 2:
                    activate2(c - 2)
                keep_diagonals(c)
            act.wait_ge(pairs_act, FILLS * CHUNKS)
            for j in range(BLOCKS):
                act.wait_ge(pairs_in[j], 16 * (CHUNKS - 1))
            for strip in (0, 1):
                store_strip(act, strip)
            activate1(CHUNKS - 2)
            act.wait_ge(pairs_out, 16 * STRIPS * CHUNKS)
            load_block(act, 1)
            activate2(CHUNKS - 2)
            activate1(CHUNKS - 1)
            activate2(CHUNKS - 1)

        @block.vector
        def _(dve):
            def make_select(i):
                dve.wait_ge(ids_rep_in[i % RAW], 16 * (i // RAW + 1))
                if i >= 2:
                    dve.wait_ge(table_used, i - 1)
                for k in range(KS):
                    nc.vector.tensor_scalar(select[i % 2][:, k, :], ids_rep[:, i % RAW, :], row_id[:, k:k + 1],
                                            None, ALU.is_equal).then_inc(select_done, 1)

            def split(i):
                dve.wait_ge(hi_done, i + 1)
                nc.vector.tensor_tensor(table_lo[i % 2][:, :, :], table[:, i % RAW, :, :],
                                        table_hi[i % 2][:, :, :].bitcast(fp32), ALU.subtract).then_inc(lo_done, 1)

            def keep_diagonals(c):
                for n in range(FILLS):
                    dve.wait_ge(fill_done, FILLS * c + n + 1)
                    if n == 0 and c >= 1:
                        dve.wait_ge(pairs_out, 16 * STRIPS * c)
                    fill_to_pairs(nc.vector.tensor_copy, n, 2)
                    fill_to_pairs(nc.vector.tensor_copy, n, 3).then_inc(pairs_dve, 1)

            def rectify1(c):
                dve.wait_ge(layer1_done, 2 * c + 2)
                for m in range(M1 // 2, M1):
                    op = nc.vector.tensor_scalar(h1[:, m, :], mlp[1][:, m - M1 // 2, :], b1[:, m:m + 1], 0.0,
                                                 ALU.add, ALU.max)
                op.then_inc(h1_dve, 1)

            def rectify2(c):
                dve.wait_ge(layer2_done, 2 * c + 2)
                nc.vector.tensor_scalar(h2[:, 1, :], mlp[1][:, 0, :], b2[:, 1:2], 0.0,
                                        ALU.add, ALU.max).then_inc(h2_dve, 1)

            dve.wait_ge(row_int_done, 1)
            nc.vector.tensor_copy(row_id[:, :], row_int[:, :]).then_inc(row_id_done, 1)
            dve.wait_ge(row_id_done, 1)
            for i in range(NS):
                make_select(i)
                split(i)
            nc.vector.memset(feats[:, :, FEATURES:SLOTS], 0.0).then_inc(slots_zeroed, 1)
            dve.wait_ge(dense_in, 16)
            for c in range(CHUNKS):
                now = slice(c * P, (c + 1) * P)
                nc.vector.tensor_copy(feats[:, now, 0].rearrange("d (t s) -> d t s", s=STRIPS),
                                      dense[:, now].rearrange("d (s t) -> d t s", s=STRIPS)).then_inc(dense_placed, 1)
            dve.wait_ge(w1d_in, 16)
            nc.vector.tensor_tensor(w1d_sum[:, :], w1d[:, 0, :], w1d[:, 1, :], ALU.add).then_inc(w1_summed, 1)
            keep_diagonals(0)
            dve.wait_ge(small_in, 48)
            for c in range(1, CHUNKS):
                if c >= 2:
                    rectify1(c - 2)
                    rectify2(c - 2)
                keep_diagonals(c)
            for c in range(CHUNKS - 2, CHUNKS):
                rectify1(c)
                rectify2(c)

        @block.tensor
        def _(pe):
            def look_up(i):
                pe.wait_ge(hi_done, i + 1)
                if i >= 4:
                    pe.wait_ge(table_placed, i - 3)
                for k in range(KS):
                    pe.wait_ge(select_done, KS * i + k + 1)
                    nc.tensor.matmul(looked_up[i % 4], table_hi[i % 2][:, k, :], select[i % 2][:, k, :],
                                     start=(k == 0), stop=False)
                pe.wait_ge(lo_done, i + 1)
                for k in range(KS):
                    op = nc.tensor.matmul(looked_up[i % 4], table_lo[i % 2][:, k, :], select[i % 2][:, k, :],
                                          start=False, stop=(k == KS - 1))
                op.then_inc(table_used, 1)

            def turn(n):
                c, g = turns[n]
                if n >= 2:
                    pe.wait_ge(group_placed, n - 1)
                for i in range(SIZES[g]):
                    pe.wait_ge(gathered[c % 2][STARTS[g] + i], 16 * (c // 2 + 1))
                    op = nc.tensor.transpose(turned[n % 2][:, i, :], rows[:, c % 2, STARTS[g] + i, :], ident[:, :])
                op.then_inc(group_turned, 1)

            def grams(c):
                pe.wait_ge(group_placed, GROUPS * (c + 1))
                if c == 0:
                    pe.wait_ge(table_placed, NS)
                    pe.wait_ge(dense_placed, CHUNKS)
                    pe.wait_ge(slots_zeroed, 1)
                for n in range(FILLS):
                    if FILLS * c + n >= 2:
                        pe.wait_ge(pairs_act, FILLS * c + n - 1)
                        pe.wait_ge(pairs_dve, FILLS * c + n - 1)
                    for k in range(FILL_COLS):
                        at = c * P + (n * FILL_COLS + k) * STRIPS
                        four = feats[:, at:at + STRIPS, :]
                        op = nc.tensor.matmul(gram[n % 2][:, k, :, 0:FEATURES], four.rearrange("d s f -> d (s f)"),
                                              four[:, :, 0:FEATURES], start=True, stop=True)
                    op.then_inc(fill_done, 1)

            def layer1(c):
                if c == 0:
                    pe.wait_ge(w1_summed, 1)
                    pe.wait_ge(w1p_in, 16)
                    pe.wait_ge(w2_in, 16)
                    pe.wait_ge(small_in, 48)
                else:
                    pe.wait_ge(y_done, c)
                operands = [(w1d_sum[:, :], dense[:, c * P:(c + 1) * P])]
                operands += [(w1p[:, j, :], pair_rows[:, j, :]) for j in range(BLOCKS)]
                for k, (weights, moving) in enumerate(operands):
                    if k >= 1:
                        pe.wait_ge(pairs_in[k - 1], 16 * (c + 1))
                    for m in range(M1):
                        op = nc.tensor.matmul(mlp[m // 2][:, m % 2, :], weights[:, m * P:(m + 1) * P], moving,
                                              start=(k == 0 and m % 2 == 0), stop=(k == BLOCKS),
                                              skip_group_check=True)
                        if k == BLOCKS and m % 2:
                            op.then_inc(layer1_done, 1)

            def layer2(c):
                pe.wait_ge(h1_act, c + 1)
                pe.wait_ge(h1_dve, c + 1)
                for m in range(M2):
                    for k in range(M1):
                        op = nc.tensor.matmul(mlp[m][:, 0, :], w2[:, k, m * P:(m + 1) * P], h1[:, k, :],
                                              start=(k == 0), stop=(k == M1 - 1))
                    op.then_inc(layer2_done, 1)

            def layer3(c):
                pe.wait_ge(h2_act, c + 1)
                pe.wait_ge(h2_dve, c + 1)
                for k in range(M2):
                    op = nc.tensor.matmul(mlp[0][0:1, 0, :], w3[:, k:k + 1], h2[:, k, :],
                                          start=(k == 0), stop=(k == M2 - 1))
                op.then_inc(layer3_done, 1)

            pe.wait_ge(ident_done, 2)
            for i in range(max(NS, FIRST_GRAM + 1)):
                if i < NS:
                    look_up(i)
                if i >= 1:
                    turn(i - 1)
            grams(0)
            for c in range(1, CHUNKS):
                if c >= 2:
                    layer1(c - 2)
                for g in range(GROUPS):
                    if c >= 2 and g == FIRST_PART:
                        layer2(c - 2)
                    if index_of[c, g] >= FIRST_GRAM:
                        turn(index_of[c, g])
                if c >= 2:
                    layer3(c - 2)
                grams(c)
            for c in range(CHUNKS - 2, CHUNKS):
                layer1(c)
                layer2(c)
                layer3(c)


def kernel(**inputs):
    import numpy as np
    import concourse.bacc as bacc
    from concourse import mybir
    from concourse.bass_utils import run_bass_kernel_spmd

    w1 = np.asarray(inputs["W_top1"])
    w2 = np.asarray(inputs["W_top2"])
    x = np.asarray(inputs["r_dense_features"])
    ids = np.asarray(inputs["ids"])
    batch, d = x.shape
    n_pairs = FEATURES * (FEATURES - 1) // 2
    h1, h2 = w2.shape
    w1_places = np.stack([np.zeros_like(w1[0]) if row is None else w1[d + row] for row in pair_places()])
    ids_cts = ids.reshape(batch // P, STRIPS, P // STRIPS, TABLES).transpose(0, 2, 1, 3)
    ks = -(-ROWS_SELECTED // P)
    table_rows = np.stack([
        np.concatenate([np.asarray(inputs[f"tbl_{f}"]), np.zeros((ks * P - ROWS_SELECTED, d), np.float32)])
        for f in SELECTED]).reshape(len(SELECTED), P, ks, d)
    arrays = {
        "dense_t": x.T,
        "ids_gather": ids_cts[..., GATHERED].reshape(batch // P, P, -1).transpose(1, 0, 2).reshape(P, -1),
        "ids_select": ids_cts[..., SELECTED].reshape(batch, -1).T,
        "table_rows": table_rows,
        "w1_dense": np.stack([w1[0:d], w1[d + n_pairs:]], axis=1),
        "w1_pairs": w1_places.reshape(3, -1, h1).transpose(1, 0, 2),
        "b1": np.asarray(inputs["b_top1"]).reshape(h1 // P, P).T,
        "w2": w2.reshape(h1 // P, P, h2).transpose(1, 0, 2),
        "b2": np.asarray(inputs["b_top2"]).reshape(h2 // P, P).T,
        "w3": np.asarray(inputs["W_top3"]).reshape(h2 // P, P).T,
    }
    for f in GATHERED:
        arrays[f"tbl_{f}"] = np.asarray(inputs[f"tbl_{f}"])
    arrays = {f"in_{name}": np.ascontiguousarray(a) for name, a in arrays.items()}

    nc = bacc.Bacc("TRN2", target_bir_lowering=False, num_devices=1)
    aps = {name[3:]: nc.dram_tensor(name, a.shape, mybir.dt.from_np(a.dtype), kind="ExternalInput").ap()
           for name, a in arrays.items()}
    out = nc.dram_tensor("out", (1, batch), mybir.dt.float32, kind="ExternalOutput").ap()
    build_tower(nc, aps["dense_t"], aps["ids_gather"], aps["ids_select"],
                {f: aps[f"tbl_{f}"] for f in GATHERED}, aps["table_rows"], aps["w1_dense"], aps["w1_pairs"],
                aps["b1"], aps["w2"], aps["b2"], aps["w3"], out)
    result = run_bass_kernel_spmd(nc, [arrays], core_ids=[0])
    return result.results[0]["out"].reshape(batch, 1)
```

```python
import concourse.bass as bass
from concourse import mybir
from contextlib import ExitStack

SELECTED = [5, 6, 8, 10, 14, 16, 18, 19, 20]
ROWS_SELECTED = 1000
LATE = 22
LATE_FROM = 2
TABLES = 26
GATHERED = [f for f in range(TABLES) if f not in SELECTED + [LATE]] + [LATE]
FEATURES = TABLES + 1
SLOT_FEATURES = [1 + f for f in GATHERED + SELECTED] + [0]
SHIFTS = (FEATURES + 1) // 2
P = 128
STRIPS = 4


def pair_places():
    seen, places = set(), []
    for slot in range(FEATURES):
        for shift in range(1, SHIFTS + 1):
            a, b = divmod(slot * FEATURES + slot + shift, FEATURES)
            if a >= FEATURES or (min(a, b), max(a, b)) in seen:
                places.append(None)
                continue
            seen.add((min(a, b), max(a, b)))
            low, high = sorted((SLOT_FEATURES[a], SLOT_FEATURES[b]))
            places.append(low * FEATURES - low * (low + 1) // 2 + high - low - 1)
    assert len(seen) == FEATURES * (FEATURES - 1) // 2
    return places


def build_tower(nc, dense_t, ids_gather, ids_select, tables, table_rows, w1_dense, w1_pairs, b1_cols,
                w2_rows, b2_row, w3_row, out):
    fp32 = mybir.dt.float32
    fp32r = mybir.dt.float32r
    int32 = mybir.dt.int32
    ALU = mybir.AluOpType
    ACT = mybir.ActivationFunctionType

    D, B = dense_t.shape
    H1 = w1_dense.shape[2]
    H2 = w2_rows.shape[2]
    M1 = H1 // P
    CHUNKS = B // P
    COLS = P // STRIPS
    FOUR = STRIPS * FEATURES
    BLOCKS = 3
    PER_BLOCK = FEATURES // BLOCKS
    PAIR_P = PER_BLOCK * SHIFTS
    SQUARE = FEATURES + 1
    NG, NS = len(GATHERED), len(SELECTED)
    KS = table_rows.shape[2]

    GROUPS = -(-NG // 4)
    SIZES = [4] * (GROUPS - 3) + [NG - 4 * (GROUPS - 2) - 2, 4, 2]
    STARTS = [sum(SIZES[:g]) for g in range(GROUPS)]
    turns = [(c, g) for c in range(CHUNKS) for g in range(GROUPS)]
    index_of = {cg: n for n, cg in enumerate(turns)}
    FILLS, FILL_COLS = 4, 8
    HALF_COLS = FILL_COLS // 2
    QUARTER = FILL_COLS // 4
    LAST_QUARTER = FILL_COLS - QUARTER

    def group_size(n):
        c, g = turns[n]
        return SIZES[g] - (g == GROUPS - 1 and c >= LATE_FROM)

    def columns_of(i):
        return slice(LATE_FROM * P if i == NS else 0, B)

    def parts(i):
        return [slice(0, KS // 2), slice(KS // 2, KS)] if i == 0 else [slice(0, KS)]

    def parts_done(i, k=KS - 1):
        return i + 1 if i == 0 and k < KS // 2 else i + 2

    LOW_BEFORE = [[4, 6], [2]] + [[0]] * (NS - 1)
    assert KS == 8
    K_GROUPS = [[[0, 1, 2, 3], [4, 5, 7], [6]] if i == 0 else [[k] for k in range(KS)] for i in range(NS + 1)]

    FIRST_GRAM = 2 * GROUPS
    BEFORE_LAYER1 = 3
    assert GROUPS == BEFORE_LAYER1 + 2
    turned_by = [i if i < NS - 2 else FIRST_GRAM - 2 * (NS - 1 - i) for i in range(NS)]
    assert turned_by == sorted(turned_by)
    WARM_UP = 11
    RAW = 3

    ctx = ExitStack()
    with ctx:
        def sb(name, shape, dt=fp32):
            return ctx.enter_context(nc.sbuf_tensor(name, shape, dt))

        def pb(name, shape):
            return ctx.enter_context(nc.psum_tensor(name, shape, fp32))

        def sem(name):
            return ctx.enter_context(nc.semaphore(name))

        ids = sb("ids", [P, CHUNKS * NG], int32)
        ids_rep = sb("ids_rep", [P, RAW, B], int32)
        row_int = sb("row_int", [P, KS], int32)
        row_id = sb("row_id", [P, KS])
        minus_row_id = sb("minus_row_id", [P, KS])
        select = [sb(f"select{i}", [P, KS, B], fp32r) for i in range(2)]
        table = sb("table", [P, RAW, KS, D])
        table_hi = [sb(f"table_hi{i}", [P, KS, D], fp32r) for i in range(2)]
        table_lo = [sb(f"table_lo{i}", [P, KS, D], fp32r) for i in range(2)]
        rows = sb("rows", [P, 2, NG, D])
        feats = sb("feats", [D, B, FEATURES])
        dense = sb("dense", [D, B])
        products = sb("products", [FOUR, 2, FOUR, COLS])
        zeros = sb("zeros", [P, B], mybir.dt.bfloat16)
        distance = sb("distance", [P, B])
        pair_rows = sb("pair_rows", [PAIR_P, BLOCKS, P])
        ident = sb("ident", [P, P])
        w1d = sb("w1d", [D, 2, H1])
        w1d_sum = sb("w1d_sum", [D, H1])
        w1p = sb("w1p", [PAIR_P, BLOCKS, H1])
        w2 = sb("w2", [P, M1, H2])
        w3_rep = sb("w3_rep", [P, H2])
        b1 = sb("b1", [P, M1])
        b2_rep = sb("b2_rep", [P, H2])
        h1 = sb("h1", [P, M1, P])
        h2 = sb("h2", [P, H2])
        weighed = sb("weighed", [P, H2])
        y = sb("y", [P, CHUNKS])
        scratch = nc.dram_tensor("pairs_scratch", (SQUARE, FEATURES, P), fp32, kind="Internal").ap()

        turned = [pb(f"turned{i}", [D, 4, P]) for i in range(2)]
        gram = [pb(f"gram{i}", [P, FILL_COLS, P]) for i in range(2)]
        mlp = [pb(f"mlp{i}", [P, 4, P]) for i in range(2)]
        looked_up = [gram[i // 2][:, 4 * (i % 2):4 * (i % 2) + 4, :].rearrange("p k n -> p (k n)")
                     for i in range(4)]
        late_looked_up = mlp[1][:, 0:CHUNKS - LATE_FROM, :].rearrange("p k n -> p (k n)")
        layer2_place = mlp[0][:, 0:H2 // P, :].rearrange("p m n -> p (m n)")

        def looked_up_place(i):
            return late_looked_up if i == NS else looked_up[i % 4]

        ids_in = sem("ids_in")
        dense_in = sem("dense_in")
        ids_rep_in = [sem(f"ids_rep_in{i}") for i in range(RAW)]
        table_in = [sem(f"table_in{i}") for i in range(RAW)]
        first_part_in = sem("first_part_in")
        w1d_in = sem("w1d_in")
        w1p_in = sem("w1p_in")
        w2_in = sem("w2_in")
        b1_in = sem("b1_in")
        finish_in = sem("finish_in")
        ident_done = sem("ident_done")
        row_int_done = sem("row_int_done")
        row_id_done = sem("row_id_done")
        zeros_done = sem("zeros_done")
        zeros_out = sem("zeros_out")
        w1_summed = sem("w1_summed")
        gathered = [[sem(f"gathered{half}_{n}") for n in range(NG)] for half in range(2)]
        hi_done = sem("hi_done")
        lo_done = sem("lo_done")
        select_done = sem("select_done")
        distance_done = sem("distance_done")
        select_act = sem("select_act")
        table_used = sem("table_used")
        table_placed = sem("table_placed")
        group_turned = sem("group_turned")
        placed_act = sem("placed_act")
        placed_dve = sem("placed_dve")
        dense_placed = sem("dense_placed")
        fill_done = sem("fill_done")
        kept_act = sem("kept_act")
        kept_dve = sem("kept_dve")
        pairs_out = sem("pairs_out")
        pairs_in = [sem(f"pairs_in{j}") for j in range(BLOCKS)]
        last_strip_out = sem("last_strip_out")
        last_block_in = sem("last_block_in")
        layer1_done = sem("layer1_done")
        h1_act = sem("h1_act")
        h1_dve = sem("h1_dve")
        layer2_done = sem("layer2_done")
        h2_done = sem("h2_done")
        y_done = sem("y_done")
        out_stored = sem("out_stored")

        def layer1_place(c, m):
            if c == CHUNKS - 1:
                return looked_up[m][:, 0:P]
            return (mlp if c < CHUNKS - 2 else turned)[m % 2][:, m // 2, :]

        def tile_order(c):
            return [*range(0, M1, 2), *range(1, M1, 2)] if c < CHUNKS - 1 else range(M1)

        def layer1_tiles_done(c, m):
            return M1 * c + (M1 // 2 * (m % 2 + 1) if c < CHUNKS - 1 else m + 1)

        block = ctx.enter_context(nc.Block())

        def store_strip(engine, c, strip):
            own = slice(FEATURES * strip, FEATURES * (strip + 1))
            return engine.dma_start(scratch[0:FEATURES, :, strip * COLS:(strip + 1) * COLS],
                                    products[own, c % 2, own, :])

        def load_block(engine, j):
            source = bass.AP(scratch.tensor, (PER_BLOCK * j * (FEATURES + 1) + 1) * P,
                             [[(FEATURES + 1) * P, PER_BLOCK], [P, SHIFTS], [1, P]])
            return engine.dma_start(pair_rows[:, j, :], source)

        def keep_half(engine_copy, c, n, half):
            at = n * FILL_COLS + half * HALF_COLS
            return engine_copy(products[:, c % 2, :, at:at + HALF_COLS].rearrange("p q t -> p t q"),
                               gram[n % 2][0:FOUR, half * HALF_COLS:(half + 1) * HALF_COLS, 0:FOUR])

        def gram_place(c, n, k):
            if (c, n) == (CHUNKS - 1, FILLS - 1) and k >= LAST_QUARTER:
                return (n + 1) % 2, k - LAST_QUARTER
            return n % 2, k

        def last_columns(engine_copy, k):
            fill, column = gram_place(CHUNKS - 1, FILLS - 1, k)
            at = (FILLS - 1) * FILL_COLS + k
            return engine_copy(products[:, (CHUNKS - 1) % 2, :, at:at + QUARTER].rearrange("p q t -> p t q"),
                               gram[fill][0:FOUR, column:column + QUARTER, 0:FOUR])

        def group_to_feats(engine_copy, n):
            c, g = turns[n]
            lo, size = STARTS[g], group_size(n)
            return engine_copy(feats[:, c * P:(c + 1) * P, lo:lo + size].rearrange("d b f -> d f b"),
                               turned[n % 2][:, 0:size, :])

        def on_vector(n):
            return n >= FIRST_GRAM and turns[n][1] % 2 == 0

        def wait_placed(engine, n):
            engine.wait_ge(placed_act, sum(not on_vector(i) for i in range(n + 1)))
            if any(on_vector(i) for i in range(n + 1)):
                engine.wait_ge(placed_dve, sum(on_vector(i) for i in range(n + 1)))

        @block.sync
        def _(sp):
            sp.dma_start(ids[:, :], ids_gather).then_inc(ids_in, 16)
            for i in range(NS + 1):
                now = columns_of(i)
                everywhere = ids_select[i:i + 1, now].broadcast_to([P, now.stop - now.start])
                if i >= RAW:
                    sp.wait_ge(lo_done, parts_done(i - RAW))
                    sp.wait_ge(select_done, (KS - 1) * (i - RAW + 1))
                    sp.wait_ge(select_act, i - RAW + 1)
                sp.dma_start(ids_rep[:, i % RAW, now], everywhere).then_inc(ids_rep_in[i % RAW], 16)
                for ks in parts(i):
                    come = first_part_in if ks.stop < KS else table_in[i % RAW]
                    sp.dma_start(table[:, i % RAW, ks, :], table_rows[i, :, ks, :]).then_inc(come, 16)
                if i == RAW:
                    sp.dma_start(dense[:, :], dense_t).then_inc(dense_in, 16)
            sp.dma_start(w1p[:, :, :], w1_pairs).then_inc(w1p_in, 16)
            sp.dma_start(w1d[:, :, :], w1_dense).then_inc(w1d_in, 16)
            sp.dma_start(w2[:, :, :], w2_rows).then_inc(w2_in, 16)
            sp.dma_start(b1[:, :], b1_cols).then_inc(b1_in, 16)
            sp.wait_ge(zeros_done, 1)
            sp.dma_start(scratch[FEATURES, 0:SHIFTS, :],
                         zeros[0:SHIFTS, 0:2 * P].bitcast(fp32)).then_inc(zeros_out, 16)
            sp.wait_ge(zeros_out, 16)
            for c in range(CHUNKS):
                last = c == CHUNKS - 1
                if c >= 1:
                    for j in range(BLOCKS):
                        sp.wait_ge(pairs_in[j], 16 * c)
                sp.wait_ge(kept_act, FILLS * (c + 1) + last)
                sp.wait_ge(kept_dve, FILLS * (c + 1))
                for strip in range(STRIPS - last):
                    store_strip(sp, c, strip).then_inc(pairs_out, 16)
                if c >= 1:
                    sp.wait_ge(layer1_done, M1 * c)
                sp.wait_ge(pairs_out, 16 * (STRIPS * (c + 1) - last))
                if last:
                    sp.wait_ge(last_strip_out, 16)
                for j in range(BLOCKS - last):
                    load_block(sp, j).then_inc(pairs_in[j], 16)
                if c == 0:
                    sp.dma_start(b2_rep[:, :], b2_row.broadcast_to([P, H2])).then_inc(finish_in, 16)
                    sp.dma_start(w3_rep[:, :], w3_row.broadcast_to([P, H2])).then_inc(finish_in, 16)
            sp.wait_ge(y_done, CHUNKS)
            sp.dma_start(out, y[:, :]).then_inc(out_stored, 16)
            sp.wait_ge(out_stored, 16)

        @block.gpsimd
        def _(pool):
            pool.iota(row_int[:, :], [[1, KS]], base=0, channel_multiplier=KS).then_inc(row_int_done, 1)
            pool.memset(ident[:, :], 0.0).then_inc(ident_done, 1)
            pool.wait_ge(ident_done, 1)
            pool.affine_select(out=ident[:, :], in_=ident[:, :], compare_op=ALU.not_equal, fill=1.0,
                               base=0, pattern=[[-1, P]], channel_multiplier=1).then_inc(ident_done, 1)
            pool.wait_ge(ids_in, 16)
            for c in range(CHUNKS):
                for n in range(NG - (c >= LATE_FROM)):
                    if c >= 2 and n in STARTS:
                        pool.wait_ge(group_turned, index_of[c - 2, STARTS.index(n)] + 1)
                    col = c * NG + n
                    pool.indirect_dma_start(
                        rows[:, c % 2, n, :], None, tables[GATHERED[n]],
                        bass.IndirectOffsetOnAxis(ids[:, col:col + 1], 0)).then_inc(gathered[c % 2][n], 16)
            for j in range(BLOCKS):
                pool.wait_ge(pairs_in[j], 16 * (CHUNKS - 1))
            pool.wait_ge(kept_act, FILLS * CHUNKS + 1)
            pool.wait_ge(kept_dve, FILLS * CHUNKS)
            store_strip(pool, CHUNKS - 1, STRIPS - 1).then_inc(last_strip_out, 16)
            pool.wait_ge(layer1_done, M1 * (CHUNKS - 1))
            pool.wait_ge(pairs_out, 16 * (STRIPS * CHUNKS - 1))
            pool.wait_ge(last_strip_out, 16)
            load_block(pool, BLOCKS - 1).then_inc(last_block_in, 16)

        @block.scalar
        def _(act):
            def split(i):
                if i >= 2:
                    act.wait_ge(table_used, i - 1)
                for ks in parts(i):
                    if ks.stop < KS:
                        act.wait_ge(first_part_in, 16)
                    else:
                        act.wait_ge(table_in[i % RAW], 16 * (i // RAW + 1))
                    nc.scalar.copy(table_hi[i % 2][:, ks, :], table[:, i % RAW, ks, :]).then_inc(hi_done, 1)

            def select_last(i):
                act.wait_ge(ids_rep_in[i % RAW], 16 * (i // RAW + 1))
                if i >= 1:
                    act.wait_ge(select_act, i)
                now = columns_of(i)
                nc.scalar.activation(distance[:, now], ids_rep[:, i % RAW, now], ACT.Abs,
                                     bias=minus_row_id[:, KS - 1:KS]).then_inc(distance_done, 1)
                act.wait_ge(distance_done, i + 1)
                nc.scalar.activation(select[i % 2][:, KS - 1, now], distance[:, now], ACT.Relu, bias=1.0,
                                     scale=-1.0).then_inc(select_act, 1)

            def place_dense():
                act.wait_ge(dense_in, 16)
                for c in range(CHUNKS):
                    now = slice(c * P, (c + 1) * P)
                    op = nc.scalar.copy(feats[:, now, FEATURES - 1].rearrange("d (t s) -> d t s", s=STRIPS),
                                        dense[:, now].rearrange("d (s t) -> d t s", s=STRIPS))
                op.then_inc(dense_placed, 1)

            def place_table(i):
                act.wait_ge(table_used, i + 1)
                slot = NG - 1 if i == NS else NG + i
                nc.scalar.copy(feats[:, columns_of(i), slot], looked_up_place(i)).then_inc(table_placed, 1)

            def place_group(n):
                act.wait_ge(group_turned, n + 1)
                group_to_feats(nc.scalar.copy, n).then_inc(placed_act, 1)

            def keep(c):
                for n in range(FILLS):
                    act.wait_ge(fill_done, 2 * (FILLS * c + n) + 1)
                    if n == 0 and c >= 2:
                        act.wait_ge(pairs_out, 16 * STRIPS * (c - 1))
                    keep_half(nc.scalar.copy, c, n, 0).then_inc(kept_act, 1)
                if c == CHUNKS - 1:
                    act.wait_ge(fill_done, 2 * FILLS * CHUNKS + 1)
                    last_columns(nc.scalar.copy, LAST_QUARTER).then_inc(kept_act, 1)

            def activate1(c):
                for m in range(0, M1, 2):
                    act.wait_ge(layer1_done, layer1_tiles_done(c, m))
                    nc.scalar.activation(h1[:, m, :], layer1_place(c, m), ACT.Relu,
                                         bias=b1[:, m:m + 1]).then_inc(h1_act, 1)

            split(0)
            act.wait_ge(row_id_done, 2)
            select_last(0)
            split(1)
            select_last(1)
            for i in range(NS):
                place_table(i)
                if i + 2 <= NS:
                    split(i + 2)
                for n in range(turned_by[i - 1] if i else 0, turned_by[i]):
                    place_group(n)
                if i + 2 <= NS:
                    select_last(i + 2)
                if i == 4:
                    place_dense()
            keep(0)
            keep(1)
            place_table(NS)
            act.wait_ge(b1_in, 16)
            for c in range(2, CHUNKS):
                for g in range(GROUPS):
                    if g == BEFORE_LAYER1:
                        activate1(c - 2)
                    if not on_vector(index_of[c, g]):
                        place_group(index_of[c, g])
                keep(c)
            for c in range(CHUNKS - 2, CHUNKS):
                activate1(c)

        @block.vector
        def _(dve):
            def make_select(i):
                dve.wait_ge(ids_rep_in[i % RAW], 16 * (i // RAW + 1))
                if i >= 2:
                    dve.wait_ge(table_used, i - 1)
                now = columns_of(i)
                for k in range(KS - 1):
                    if k in LOW_BEFORE[i]:
                        split(i, parts(i)[LOW_BEFORE[i].index(k)])
                    nc.vector.tensor_scalar(select[i % 2][:, k, now], ids_rep[:, i % RAW, now], row_id[:, k:k + 1],
                                            None, ALU.is_equal).then_inc(select_done, 1)

            def split(i, ks):
                dve.wait_ge(hi_done, parts_done(i, ks.start))
                nc.vector.tensor_tensor(table_lo[i % 2][:, ks, :], table[:, i % RAW, ks, :],
                                        table_hi[i % 2][:, ks, :].bitcast(fp32), ALU.subtract).then_inc(lo_done, 1)

            def keep(c):
                for n in range(FILLS):
                    dve.wait_ge(fill_done, 2 * (FILLS * c + n + 1))
                    if n == 0 and c >= 2:
                        dve.wait_ge(pairs_out, 16 * STRIPS * (c - 1))
                    if c == CHUNKS - 1 and n == FILLS - 1:
                        last_columns(nc.vector.tensor_copy, HALF_COLS).then_inc(kept_dve, 1)
                    else:
                        keep_half(nc.vector.tensor_copy, c, n, 1).then_inc(kept_dve, 1)

            def place_group(n):
                dve.wait_ge(group_turned, n + 1)
                group_to_feats(nc.vector.tensor_copy, n).then_inc(placed_dve, 1)

            def rectify1(c):
                for m in range(1, M1, 2):
                    dve.wait_ge(layer1_done, layer1_tiles_done(c, m))
                    nc.vector.tensor_scalar(h1[:, m, :], layer1_place(c, m), b1[:, m:m + 1], 0.0,
                                            ALU.add, ALU.max).then_inc(h1_dve, 1)

            def finish(c):
                dve.wait_ge(finish_in, 32)
                dve.wait_ge(layer2_done, c + 1)
                nc.vector.tensor_tensor(h2[:, :], layer2_place,
                                        b2_rep[:, :], ALU.add).then_inc(h2_done, 1)
                dve.wait_ge(h2_done, c + 1)
                nc.vector.scalar_tensor_tensor(out=weighed[:, :], in0=h2[:, :], scalar=0.0, in1=w3_rep[:, :],
                                               op0=ALU.max, op1=ALU.mult,
                                               accum_out=y[:, c:c + 1]).then_inc(y_done, 1)

            nc.vector.memset(zeros[:, :], 0.0).then_inc(zeros_done, 1)
            dve.wait_ge(row_int_done, 1)
            nc.vector.tensor_copy(row_id[:, :], row_int[:, :]).then_inc(row_id_done, 1)
            nc.vector.tensor_scalar(minus_row_id[:, :], row_int[:, :], -1.0, None, ALU.mult).then_inc(row_id_done, 1)
            dve.wait_ge(row_id_done, 1)
            for i in range(NS + 1):
                make_select(i)
            dve.wait_ge(w1d_in, 16)
            nc.vector.tensor_tensor(w1d_sum[:, :], w1d[:, 0, :], w1d[:, 1, :], ALU.add).then_inc(w1_summed, 1)
            keep(0)
            keep(1)
            dve.wait_ge(b1_in, 16)
            for c in range(2, CHUNKS):
                for g in range(GROUPS):
                    if g == BEFORE_LAYER1:
                        rectify1(c - 2)
                    if on_vector(index_of[c, g]):
                        place_group(index_of[c, g])
                if c < CHUNKS - 1:
                    finish(c - 2)
                keep(c)
            finish(CHUNKS - 3)
            for c in range(CHUNKS - 2, CHUNKS):
                rectify1(c)
                finish(c)

        @block.tensor
        def _(pe):
            def look_up(i):
                if 4 <= i < NS:
                    pe.wait_ge(table_placed, i - 3)
                now = columns_of(i)
                for ks in K_GROUPS[i]:
                    for part, done in ((table_hi, hi_done), (table_lo, lo_done)):
                        for k in ks:
                            pe.wait_ge(done, parts_done(i, k))
                            if k < KS - 1:
                                pe.wait_ge(select_done, (KS - 1) * i + k + 1)
                            else:
                                pe.wait_ge(select_act, i + 1)
                            op = nc.tensor.matmul(
                                looked_up_place(i), part[i % 2][:, k, :], select[i % 2][:, k, now],
                                start=(part is table_hi and k == ks[0] == 0),
                                stop=(part is table_lo and k == ks[-1] and ks is K_GROUPS[i][-1]))
                op.then_inc(table_used, 1)

            def turn(n):
                c, g = turns[n]
                if n >= 2:
                    wait_placed(pe, n - 2)
                for i in range(group_size(n)):
                    pe.wait_ge(gathered[c % 2][STARTS[g] + i], 16 * (c // 2 + 1))
                    op = nc.tensor.transpose(turned[n % 2][:, i, :], rows[:, c % 2, STARTS[g] + i, :], ident[:, :])
                op.then_inc(group_turned, 1)

            def grams(c):
                wait_placed(pe, GROUPS * (c + 1) - 1)
                if c == 0:
                    pe.wait_ge(table_placed, NS)
                    pe.wait_ge(dense_placed, 1)
                if c == LATE_FROM:
                    pe.wait_ge(table_placed, NS + 1)
                for n in range(FILLS):
                    if FILLS * c + n >= 2:
                        pe.wait_ge(kept_act, FILLS * c + n - 1)
                        pe.wait_ge(kept_dve, FILLS * c + n - 1)
                    for k in range(FILL_COLS):
                        at = c * P + (n * FILL_COLS + k) * STRIPS
                        four = feats[:, at:at + STRIPS, :].rearrange("d s f -> d (s f)")
                        fill, column = gram_place(c, n, k)
                        if fill != n % 2:
                            pe.wait_ge(kept_act, FILLS * (c + 1) - 1)
                        op = nc.tensor.matmul(gram[fill][0:FOUR, column, 0:FOUR], four, four, start=True, stop=True)
                        if (k + 1) % HALF_COLS == 0 or (c, n, k + 1) == (CHUNKS - 1, FILLS - 1, LAST_QUARTER):
                            op.then_inc(fill_done, 1)

            def layer1(c, blocks):
                for k in blocks:
                    if k == 0:
                        if c == 0:
                            pe.wait_ge(w1_summed, 1)
                            pe.wait_ge(w1p_in, 16)
                            pe.wait_ge(w2_in, 16)
                            pe.wait_ge(table_placed, NS + 1)
                        elif c < CHUNKS - 2:
                            pe.wait_ge(h2_done, c)
                        elif c == CHUNKS - 1:
                            pe.wait_ge(kept_act, FILLS * CHUNKS + 1)
                            pe.wait_ge(kept_dve, FILLS * CHUNKS)
                        weights, moving = w1d_sum[:, :], dense[:, c * P:(c + 1) * P]
                    else:
                        if k == BLOCKS and c == CHUNKS - 1:
                            pe.wait_ge(last_block_in, 16)
                        else:
                            pe.wait_ge(pairs_in[k - 1], 16 * (c + 1))
                        weights, moving = w1p[:, k - 1, :], pair_rows[:, k - 1, :]
                    for m in tile_order(c):
                        clears = k == 0 and (m < 2 or c == CHUNKS - 1)
                        op = nc.tensor.matmul(layer1_place(c, m), weights[:, m * P:(m + 1) * P], moving,
                                              start=clears, stop=(k == BLOCKS), skip_group_check=True)
                        if k == BLOCKS:
                            op.then_inc(layer1_done, 1)

            def layer2(c, steps=range(M1)):
                if 0 in steps:
                    if c >= CHUNKS - 2:
                        pe.wait_ge(h2_done, c)
                    else:
                        pe.wait_ge(h1_act, M1 // 2 * (c + 1))
                for i in steps:
                    k = tile_order(c)[i]
                    pe.wait_ge(h1_dve if k % 2 else h1_act, M1 // 2 * c + k // 2 + 1)
                    op = nc.tensor.matmul(layer2_place, h1[:, k, :], w2[:, k, :],
                                          start=(i == 0), stop=(i == M1 - 1))
                    if i == M1 - 1:
                        op.then_inc(layer2_done, 1)

            pe.wait_ge(zeros_done, 1)
            for _ in range(WARM_UP):
                nc.tensor.matmul(mlp[1][:, :, :].rearrange("p m n -> p (m n)"), zeros[:, 0:P], zeros[:, :],
                                 start=True, stop=True)
            pe.wait_ge(ident_done, 2)
            for i in range(NS):
                look_up(i)
                for n in range(turned_by[i - 1] if i else 0, turned_by[i]):
                    turn(n)
            grams(0)
            grams(1)
            look_up(NS)
            for c in range(2, CHUNKS):
                groups = [index_of[c, g] for g in range(GROUPS)]
                for n in groups[:BEFORE_LAYER1 - 1]:
                    turn(n)
                layer1(c - 2, [0])
                turn(groups[BEFORE_LAYER1 - 1])
                layer1(c - 2, range(1, BLOCKS + 1))
                turn(groups[BEFORE_LAYER1])
                before = M1 - 1 if c < CHUNKS - 1 else 0
                layer2(c - 2, range(before))
                turn(groups[BEFORE_LAYER1 + 1])
                layer2(c - 2, [before])
                grams(c)
            layer2(CHUNKS - 3, range(1, M1))
            layer1(CHUNKS - 2, range(BLOCKS + 1))
            layer1(CHUNKS - 1, [0])
            layer2(CHUNKS - 2)
            layer1(CHUNKS - 1, range(1, BLOCKS + 1))
            layer2(CHUNKS - 1)


def kernel(**inputs):
    import numpy as np
    import concourse.bacc as bacc
    from concourse import mybir
    from concourse.bass_utils import run_bass_kernel_spmd

    w1 = np.asarray(inputs["W_top1"])
    w2 = np.asarray(inputs["W_top2"])
    x = np.asarray(inputs["r_dense_features"])
    ids = np.asarray(inputs["ids"])
    batch, d = x.shape
    n_pairs = FEATURES * (FEATURES - 1) // 2
    h1, h2 = w2.shape
    w1_places = np.stack([np.zeros_like(w1[0]) if row is None else w1[d + row] for row in pair_places()])
    ids_cts = ids.reshape(batch // P, STRIPS, P // STRIPS, TABLES).transpose(0, 2, 1, 3)
    ks = -(-ROWS_SELECTED // P)
    table_rows = np.stack([
        np.concatenate([np.asarray(inputs[f"tbl_{f}"]), np.zeros((ks * P - ROWS_SELECTED, d), np.float32)])
        for f in SELECTED + [LATE]]).reshape(-1, P, ks, d)
    arrays = {
        "dense_t": x.T,
        "ids_gather": ids_cts[..., GATHERED].reshape(batch // P, P, -1).transpose(1, 0, 2).reshape(P, -1),
        "ids_select": ids_cts[..., SELECTED + [LATE]].reshape(batch, -1).T,
        "table_rows": table_rows,
        "w1_dense": np.stack([w1[0:d], w1[d + n_pairs:]], axis=1),
        "w1_pairs": w1_places.reshape(3, -1, h1).transpose(1, 0, 2),
        "b1": np.asarray(inputs["b_top1"]).reshape(h1 // P, P).T,
        "w2": w2.reshape(h1 // P, P, h2).transpose(1, 0, 2),
        "b2": np.asarray(inputs["b_top2"]).reshape(1, h2),
        "w3": np.asarray(inputs["W_top3"]).reshape(1, h2),
    }
    for f in GATHERED:
        arrays[f"tbl_{f}"] = np.asarray(inputs[f"tbl_{f}"])
    arrays = {f"in_{name}": np.ascontiguousarray(a) for name, a in arrays.items()}

    nc = bacc.Bacc("TRN2", target_bir_lowering=False, num_devices=1)
    aps = {name[3:]: nc.dram_tensor(name, a.shape, mybir.dt.from_np(a.dtype), kind="ExternalInput").ap()
           for name, a in arrays.items()}
    out = nc.dram_tensor("out", (P, batch // P), mybir.dt.float32, kind="ExternalOutput").ap()
    build_tower(nc, aps["dense_t"], aps["ids_gather"], aps["ids_select"],
                {f: aps[f"tbl_{f}"] for f in GATHERED}, aps["table_rows"], aps["w1_dense"], aps["w1_pairs"],
                aps["b1"], aps["w2"], aps["b2"], aps["w3"], out)
    result = run_bass_kernel_spmd(nc, [arrays], core_ids=[0])
    return result.results[0]["out"].T.reshape(batch, 1)
```
